# Optimizing a Trainium2 kernel written in Bass

```python
import numpy as np
import jax
import jax.numpy as jnp

def _softmax(x, axis=-1):
    return jax.nn.softmax(x, axis=axis)

def _gelu(x):
    return jax.nn.gelu(x, approximate=True)

def _silu(x):
    return jax.nn.silu(x)

def _sigmoid(x):
    return jax.nn.sigmoid(x)

def _layernorm(x, axis=-1, eps=1e-05):
    m = jnp.mean(x, axis=axis, keepdims=True)
    v = jnp.var(x, axis=axis, keepdims=True)
    return (x - m) / jnp.sqrt(v + eps)

def _scatter_add(tgt, idx, src, axis=0):
    return tgt.at[idx].add(src)

def _segment_sum(src, seg, n):
    return jax.ops.segment_sum(src, seg, n)
kernel_name = 'mk_gnn_preln_d4_gnn_r8_20fe96'

def setup_inputs(seed: int=0):
    np.random.seed(seed)
    _w = jnp.asarray

    def _rec_inputs():
        import jax
        import jax.numpy as jnp
        _gk = jax.random.key(seed)
        x = -0.000202 + 1 * jax.random.normal(jax.random.fold_in(_gk, 1), (6250, 128), jnp.float32)
        _s = jax.random.randint(jax.random.fold_in(_gk, 2), (50000,), 0, 6250, jnp.int32)
        _d = jax.random.randint(jax.random.fold_in(_gk, 3), (50000,), 0, 6250, jnp.int32)
        _loop = jnp.arange(6250, dtype=jnp.int32)
        src = jnp.concatenate([_s, _d, _loop])
        dst = jnp.concatenate([_d, _s, _loop])
        _o = jnp.argsort(dst, stable=True)
        src = src[_o]
        dst = dst[_o]
        return (x, src, dst)
    x, src, dst = _rec_inputs()

    def _L0_gnn_setup():
        import jax, jax.numpy as jnp
        import numpy as np
        N_NODES = 6250
        N_EDGES = 100000
        IN_CH = 128
        OUT_CH = 128
        MLP_HID = 64
        key = jax.random.key(seed)
        ks = jax.random.split(key, 8)
        x = jax.random.normal(ks[0], (N_NODES, IN_CH), dtype=jnp.float32)
        edge_index = jax.random.randint(ks[1], (2, N_EDGES), 0, N_NODES, dtype=jnp.int64)
        s1 = 1.0 / np.sqrt(2 * IN_CH)
        mlp_w1 = jax.random.uniform(ks[2], (2 * IN_CH, MLP_HID), jnp.float32, -s1, s1)
        mlp_b1 = jax.random.uniform(ks[3], (MLP_HID,), jnp.float32, -s1, s1)
        s2 = 1.0 / np.sqrt(MLP_HID)
        mlp_w2 = jax.random.uniform(ks[4], (MLP_HID, 1), jnp.float32, -s2, s2)
        mlp_b2 = jax.random.uniform(ks[5], (1,), jnp.float32, -s2, s2)
        s3 = 1.0 / np.sqrt(IN_CH)
        conv_w = jax.random.uniform(ks[6], (IN_CH, OUT_CH), jnp.float32, -s3, s3)
        conv_b = jnp.zeros((OUT_CH,), jnp.float32)
        return {'x': x, 'edge_index': edge_index, 'mlp_w1': mlp_w1, 'mlp_b1': mlp_b1, 'mlp_w2': mlp_w2, 'mlp_b2': mlp_b2, 'conv_w': conv_w, 'conv_b': conv_b}
    _L0_gnn_all = _L0_gnn_setup()
    _L0_gnn_in = {k: v for k, v in _L0_gnn_all.items() if k in ('mlp_w1', 'mlp_b1', 'mlp_w2', 'mlp_b2', 'conv_w', 'conv_b')}
    del _L0_gnn_all

    def _L1_gnn_setup():
        import jax, jax.numpy as jnp
        import numpy as np
        N_NODES = 6250
        N_EDGES = 100000
        IN_CH = 128
        HID_CH = 256
        OUT_CH = 128

        def _gcn_norm(edge_index, num_nodes):
            loop = jnp.arange(num_nodes, dtype=edge_index.dtype)
            src = jnp.concatenate([edge_index[0], loop])
            dst = jnp.concatenate([edge_index[1], loop])
            deg = jax.ops.segment_sum(jnp.ones_like(dst, dtype=jnp.float32), dst, num_segments=num_nodes)
            dis = jnp.where(deg > 0, jax.lax.rsqrt(deg), 0.0)
            norm = dis[src] * dis[dst]
            return (src, dst, norm)

        def _gcn_conv(x, W, b, src, dst, norm, num_nodes):
            h = x @ W
            msg = h[src] * norm[:, None]
            out = jax.ops.segment_sum(msg, dst, num_segments=num_nodes)
            return out + b
        key = jax.random.key(seed)
        ks = jax.random.split(key, 8)
        x = jax.random.normal(ks[0], (N_NODES, IN_CH), dtype=jnp.float32)
        edge_index = jax.random.randint(ks[1], (2, N_EDGES), 0, N_NODES, dtype=jnp.int64)
        batch = jnp.zeros((N_NODES,), dtype=jnp.int64)
        W1 = jax.random.normal(ks[2], (IN_CH, HID_CH), dtype=jnp.float32) / np.sqrt(IN_CH)
        b1 = jnp.zeros((HID_CH,), dtype=jnp.float32)
        W2 = jax.random.normal(ks[3], (HID_CH, OUT_CH), dtype=jnp.float32) / np.sqrt(HID_CH)
        b2 = jnp.zeros((OUT_CH,), dtype=jnp.float32)
        return {'x': x, 'edge_index': edge_index, 'batch': batch, 'W1': W1, 'b1': b1, 'W2': W2, 'b2': b2}
    _L1_gnn_all = _L1_gnn_setup()
    _L1_gnn_in = {k: v for k, v in _L1_gnn_all.items() if k in ('W1', 'b1', 'W2', 'b2')}
    del _L1_gnn_all

    def _L2_gnn_setup():
        import jax, jax.numpy as jnp
        import numpy as np
        N_NODES = 12500
        N_EDGES = 75000
        D = 128
        H = 256
        key = jax.random.key(seed)
        ks = jax.random.split(key, 8)
        nodes = jax.random.normal(ks[0], (N_NODES, D), dtype=jnp.float32)
        senders = jax.random.randint(ks[1], (N_EDGES,), 0, N_NODES)
        receivers = jax.random.randint(ks[2], (N_EDGES,), 0, N_NODES)
        s = 0.05
        return {'nodes': nodes, 'senders': senders, 'receivers': receivers, 'Wm1': jax.random.normal(ks[3], (D, H), dtype=jnp.float32) * s, 'bm1': jnp.zeros((H,), dtype=jnp.float32), 'Wm2': jax.random.normal(ks[4], (H, D), dtype=jnp.float32) * s, 'bm2': jnp.zeros((D,), dtype=jnp.float32), 'Wn1': jax.random.normal(ks[5], (2 * D, H), dtype=jnp.float32) * s, 'bn1': jnp.zeros((H,), dtype=jnp.float32), 'Wn2': jax.random.normal(ks[6], (H, D), dtype=jnp.float32) * s, 'bn2': jnp.zeros((D,), dtype=jnp.float32)}
    _L2_gnn_all = _L2_gnn_setup()
    _L2_gnn_in = {k: v for k, v in _L2_gnn_all.items() if k in ('Wm1', 'bm1', 'Wm2', 'bm2', 'Wn1', 'bn1', 'Wn2', 'bn2')}
    del _L2_gnn_all

    def _L3_gnn_setup():
        import jax, jax.numpy as jnp
        import numpy as np
        N_NODES = 12500
        N_EDGES = 200000
        D_IN = 128
        D_HID = 128
        D_OUT = 128

        def _gcn_norm(edge_index, n_nodes):
            loop = jnp.arange(n_nodes, dtype=edge_index.dtype)
            src = jnp.concatenate([edge_index[0], loop])
            dst = jnp.concatenate([edge_index[1], loop])
            deg = jax.ops.segment_sum(jnp.ones_like(dst, dtype=jnp.float32), dst, num_segments=n_nodes)
            dinv = jnp.where(deg > 0, jax.lax.rsqrt(deg), 0.0)
            norm = dinv[src] * dinv[dst]
            return (src, dst, norm)

        def _gcn_conv(x, W, b, src, dst, norm, n_nodes):
            h = x @ W
            msg = h[src] * norm[:, None]
            out = jax.ops.segment_sum(msg, dst, num_segments=n_nodes)
            return out + b
        key = jax.random.key(seed)
        ks = jax.random.split(key, 8)
        x = jax.random.normal(ks[0], (N_NODES, D_IN), dtype=jnp.float32)
        edge_index = jax.random.randint(ks[1], (2, N_EDGES), 0, N_NODES, dtype=jnp.int64)

        def glorot(k, fan_in, fan_out):
            s = jnp.sqrt(6.0 / (fan_in + fan_out)).astype(jnp.float32)
            return jax.random.uniform(k, (fan_in, fan_out), jnp.float32, -s, s)
        return {'x': x, 'edge_index': edge_index, 'W0': glorot(ks[2], D_IN, D_HID), 'b0': jnp.zeros((D_HID,), jnp.float32), 'W1': glorot(ks[3], D_HID, D_HID), 'b1': jnp.zeros((D_HID,), jnp.float32), 'W2': glorot(ks[4], D_HID, D_OUT), 'b2': jnp.zeros((D_OUT,), jnp.float32)}
    _L3_gnn_all = _L3_gnn_setup()
    _L3_gnn_in = {k: v for k, v in _L3_gnn_all.items() if k in ('W0', 'b0', 'W1', 'b1', 'W2', 'b2')}
    del _L3_gnn_all
    return {'x': x, 'src': src, 'dst': dst, 'L0_gnn_mlp_w1': _L0_gnn_in['mlp_w1'], 'L0_gnn_mlp_b1': _L0_gnn_in['mlp_b1'], 'L0_gnn_mlp_w2': _L0_gnn_in['mlp_w2'], 'L0_gnn_mlp_b2': _L0_gnn_in['mlp_b2'], 'L0_gnn_conv_w': _L0_gnn_in['conv_w'], 'L0_gnn_conv_b': _L0_gnn_in['conv_b'], 'L1_gnn_W1': _L1_gnn_in['W1'], 'L1_gnn_b1': _L1_gnn_in['b1'], 'L1_gnn_W2': _L1_gnn_in['W2'], 'L1_gnn_b2': _L1_gnn_in['b2'], 'L2_gnn_Wm1': _L2_gnn_in['Wm1'], 'L2_gnn_bm1': _L2_gnn_in['bm1'], 'L2_gnn_Wm2': _L2_gnn_in['Wm2'], 'L2_gnn_bm2': _L2_gnn_in['bm2'], 'L2_gnn_Wn1': _L2_gnn_in['Wn1'], 'L2_gnn_bn1': _L2_gnn_in['bn1'], 'L2_gnn_Wn2': _L2_gnn_in['Wn2'], 'L2_gnn_bn2': _L2_gnn_in['bn2'], 'L3_gnn_W0': _L3_gnn_in['W0'], 'L3_gnn_b0': _L3_gnn_in['b0'], 'L3_gnn_W1': _L3_gnn_in['W1'], 'L3_gnn_b1': _L3_gnn_in['b1'], 'L3_gnn_W2': _L3_gnn_in['W2'], 'L3_gnn_b2': _L3_gnn_in['b2']}

def reference(x, src, dst, L0_gnn_mlp_w1, L0_gnn_mlp_b1, L0_gnn_mlp_w2, L0_gnn_mlp_b2, L0_gnn_conv_w, L0_gnn_conv_b, L1_gnn_W1, L1_gnn_b1, L1_gnn_W2, L1_gnn_b2, L2_gnn_Wm1, L2_gnn_bm1, L2_gnn_Wm2, L2_gnn_bm2, L2_gnn_Wn1, L2_gnn_bn1, L2_gnn_Wn2, L2_gnn_bn2, L3_gnn_W0, L3_gnn_b0, L3_gnn_W1, L3_gnn_b1, L3_gnn_W2, L3_gnn_b2):
    import jax
    import jax.numpy as jnp

    def _L0_gnn_ref(x, edge_index, mlp_w1, mlp_b1, mlp_w2, mlp_b2, conv_w, conv_b):
        import jax, jax.numpy as jnp
        import numpy as np
        N_NODES = 6250
        N_EDGES = 100000
        IN_CH = 128
        OUT_CH = 128
        MLP_HID = 64
        n = x.shape[0]
        row, col = (edge_index[0], edge_index[1])
        edge_feat = jnp.concatenate([x[row], x[col]], axis=-1)
        h = jax.nn.gelu(edge_feat @ mlp_w1 + mlp_b1, approximate=False)
        edge_weight = jax.nn.sigmoid(h @ mlp_w2 + mlp_b2)[:, 0]
        loop = jnp.arange(n, dtype=row.dtype)
        row_f = jnp.concatenate([row, loop])
        col_f = jnp.concatenate([col, loop])
        ew_f = jnp.concatenate([edge_weight, jnp.ones((n,), x.dtype)])
        deg = jax.ops.segment_sum(ew_f, col_f, num_segments=n)
        dinv = jnp.where(deg > 0, jax.lax.rsqrt(deg), 0.0)
        norm = dinv[row_f] * ew_f * dinv[col_f]
        xt = x @ conv_w
        msg = xt[row_f] * norm[:, None]
        out = jax.ops.segment_sum(msg, col_f, num_segments=n)
        return out + conv_b

    def _L1_gnn_ref(x, edge_index, batch, W1, b1, W2, b2):
        import jax, jax.numpy as jnp
        import numpy as np
        N_NODES = 6250
        N_EDGES = 100000
        IN_CH = 128
        HID_CH = 256
        OUT_CH = 128

        def _gcn_norm(edge_index, num_nodes):
            loop = jnp.arange(num_nodes, dtype=edge_index.dtype)
            src = jnp.concatenate([edge_index[0], loop])
            dst = jnp.concatenate([edge_index[1], loop])
            deg = jax.ops.segment_sum(jnp.ones_like(dst, dtype=jnp.float32), dst, num_segments=num_nodes)
            dis = jnp.where(deg > 0, jax.lax.rsqrt(deg), 0.0)
            norm = dis[src] * dis[dst]
            return (src, dst, norm)

        def _gcn_conv(x, W, b, src, dst, norm, num_nodes):
            h = x @ W
            msg = h[src] * norm[:, None]
            out = jax.ops.segment_sum(msg, dst, num_segments=num_nodes)
            return out + b
        n = x.shape[0]
        src, dst, norm = _gcn_norm(edge_index, n)
        h = jax.nn.relu(_gcn_conv(x, W1, b1, src, dst, norm, n))
        h = jax.nn.relu(_gcn_conv(h, W2, b2, src, dst, norm, n))
        return h

    def _L2_gnn_ref(nodes, senders, receivers, Wm1, bm1, Wm2, bm2, Wn1, bn1, Wn2, bn2):
        import jax, jax.numpy as jnp
        import numpy as np
        N_NODES = 12500
        N_EDGES = 75000
        D = 128
        H = 256
        m = jax.nn.relu(nodes @ Wm1 + bm1) @ Wm2 + bm2
        agg = jax.ops.segment_sum(m[senders], receivers, num_segments=nodes.shape[0])
        h = jnp.concatenate([nodes, agg], axis=-1)
        upd = jax.nn.relu(h @ Wn1 + bn1) @ Wn2 + bn2
        return nodes + upd

    def _L3_gnn_ref(x, edge_index, W0, b0, W1, b1, W2, b2):
        import jax, jax.numpy as jnp
        import numpy as np
        N_NODES = 12500
        N_EDGES = 200000
        D_IN = 128
        D_HID = 128
        D_OUT = 128

        def _gcn_norm(edge_index, n_nodes):
            loop = jnp.arange(n_nodes, dtype=edge_index.dtype)
            src = jnp.concatenate([edge_index[0], loop])
            dst = jnp.concatenate([edge_index[1], loop])
            deg = jax.ops.segment_sum(jnp.ones_like(dst, dtype=jnp.float32), dst, num_segments=n_nodes)
            dinv = jnp.where(deg > 0, jax.lax.rsqrt(deg), 0.0)
            norm = dinv[src] * dinv[dst]
            return (src, dst, norm)

        def _gcn_conv(x, W, b, src, dst, norm, n_nodes):
            h = x @ W
            msg = h[src] * norm[:, None]
            out = jax.ops.segment_sum(msg, dst, num_segments=n_nodes)
            return out + b
        n = x.shape[0]
        src, dst, norm = _gcn_norm(edge_index, n)
        h = jax.nn.relu(_gcn_conv(x, W0, b0, src, dst, norm, n))
        h = jax.nn.relu(_gcn_conv(h, W1, b1, src, dst, norm, n))
        return _gcn_conv(h, W2, b2, src, dst, norm, n)
    edge_index = jnp.stack([src, dst])
    batch0 = jnp.zeros((6250,), jnp.int32)
    h = jnp.maximum(_layernorm(x, axis=-1), 0.0)
    x = x + _L0_gnn_ref(h, edge_index, L0_gnn_mlp_w1, L0_gnn_mlp_b1, L0_gnn_mlp_w2, L0_gnn_mlp_b2, L0_gnn_conv_w, L0_gnn_conv_b)
    h = jnp.maximum(_layernorm(x, axis=-1), 0.0)
    x = x + _L1_gnn_ref(h, edge_index, batch0, L1_gnn_W1, L1_gnn_b1, L1_gnn_W2, L1_gnn_b2)
    h = jnp.maximum(_layernorm(x, axis=-1), 0.0)
    x = x + _L2_gnn_ref(h, src, dst, L2_gnn_Wm1, L2_gnn_bm1, L2_gnn_Wm2, L2_gnn_bm2, L2_gnn_Wn1, L2_gnn_bn1, L2_gnn_Wn2, L2_gnn_bn2)
    h = jnp.maximum(_layernorm(x, axis=-1), 0.0)
    x = x + _L3_gnn_ref(h, edge_index, L3_gnn_W0, L3_gnn_b0, L3_gnn_W1, L3_gnn_b1, L3_gnn_W2, L3_gnn_b2)
    return x

_drawn_inputs = setup_inputs


def setup_inputs(seed=0):
    import zlib

    import numpy as np

    out = dict(_drawn_inputs(seed))
    spreads = {'L0_gnn_conv_b': (0.0, 0.1),
     'L1_gnn_b1': (0.0, 0.1),
     'L1_gnn_b2': (0.0, 0.1),
     'L2_gnn_bm1': (0.0, 0.1),
     'L2_gnn_bm2': (0.0, 0.1),
     'L2_gnn_bn1': (0.0, 0.34),
     'L2_gnn_bn2': (0.0, 0.1),
     'L3_gnn_b0': (0.0, 0.477),
     'L3_gnn_b1': (0.0, 0.295),
     'L3_gnn_b2': (0.0, 0.1)}
    factors = {'L0_gnn_mlp_w1': 8.0, 'L0_gnn_mlp_b1': 8.0, 'L0_gnn_mlp_w2': 8.0}
    for name, (base, spread) in spreads.items():
        noise = np.random.default_rng([zlib.crc32(name.encode()), seed]).standard_normal(out[name].shape)
        drawn = base * np.exp(spread * noise) if base else spread * noise
        out[name] = jnp.asarray(drawn.astype(out[name].dtype))
    for name, factor in factors.items():
        out[name] = (out[name] * factor).astype(out[name].dtype)
    return out
```

```python
import concourse.bass as bass
from concourse import mybir
from contextlib import ExitStack

P = 128
N = 6250
E = 106250
D = 128
MH = 64
HID = 256
EPS = 1e-5

WB = 2
WIN_SHIFT = 8
WIN = WB * P
NW = -(-N // WIN)
NB = NW * WB
CB = 5
NC = NB // CB
CN = CB * P

T = -(-E // P)
TC = -(-T // P)
TPAD = TC * P
STEPS = T + NW - 1
S = 4
RING = 4
HELD = 2 * RING
GROUPS = -(-STEPS // S)
KPAD = TPAD
FAR = 1 << 20

PARTS = 3
PASSES = 8
USES = [len(range(j, GROUPS, RING)) for j in range(RING)]
assert NB % CB == 0 and KPAD >= GROUPS * S and 1 << WIN_SHIFT == WIN


def after(eng, sem, value):
    if not isinstance(value, int) or value > 0:
        eng.wait_ge(sem, value)


def pipeline(eng, count, unroll, stages):
    most = max(lag for lag, _ in stages)
    first = -(-(most + unroll) // unroll)
    last = count // unroll

    def turn(at, j):
        for lag, stage in stages:
            if not isinstance(at, int) or 0 <= at - lag < count:
                stage(at - lag, (j - lag) % unroll)

    for at in range(first * unroll):
        turn(at, at % unroll)
    with eng.Fori(first, last) as i:
        for j in range(unroll):
            turn(i * unroll + j, j)
    for at in range(last * unroll, count + most):
        turn(at, at % unroll)


class Own:

    def __init__(self, eng, sem):
        self.eng, self.sem, self.per, self.n = eng, sem, None, 0

    def item(self, i):
        if not isinstance(i, int) or i > 0:
            self.per = self.n if self.per is None else self.per
            assert self.n == self.per
        self.base, self.n = i * self.per if self.per else 0, 0

    def done(self, instruction):
        instruction.then_inc(self.sem, 1)
        self.n += 1

    def wait(self):
        self.eng.wait_ge(self.sem, self.base + self.n)


def build(nc, a, out):
    f32, i32, bf16 = mybir.dt.float32, mybir.dt.int32, mybir.dt.bfloat16
    ALU, ACT, AX = mybir.AluOpType, mybir.ActivationFunctionType, mybir.AxisListType
    ENG = mybir.EngineType

    table = [nc.dram_tensor("table0", (NB * P, MH), f32, kind="Internal").ap()]
    table += [nc.dram_tensor(f"table{p}", (NB * P, D), f32, kind="Internal").ap() for p in range(1, PASSES)]
    edge_list = [nc.dram_tensor(n, (TPAD, P), i32, kind="Internal").ap() for n in ("src_list", "dst_list")]

    with ExitStack() as ctx:
        def sb(name, shape, dt=f32):
            return ctx.enter_context(nc.sbuf_tensor(name, shape, dt))

        def sem(name):
            return ctx.enter_context(nc.semaphore(name))

        x = sb("x", [P, NB, D])
        h = sb("h", [P, NB, D])
        acc = sb("acc", [P, NB, D])
        dst_mlp = sb("dst_mlp", [P, NB, PARTS, MH], bf16)
        deg = sb("deg", [P, NB, PARTS + 1])
        dinv = sb("dinv", [P, 2, NB])
        deg_ok = sb("deg_ok", [P, 2, NB])

        src_of = sb("src_of", [P, KPAD], i32)
        local_dst = sb("local_dst", [P, KPAD])
        window_f = sb("window_f", [P, KPAD])
        window_of = sb("window_of", [P, KPAD], i32)
        weight = sb("weight", [P, KPAD])
        tile_of = sb("tile_of", [P, TC], i32)

        rows_i = h.ap().rearrange("p b d -> p (b d)").bitcast(i32)[:, 0:2 * TC * P].rearrange(
            "p (e c j) -> p e c j", e=2, c=TC)
        step_iota = sb("step_iota", [P, KPAD])
        tile_iota = sb("tile_iota", [P, TC])
        last_window_i = sb("last_window_i", [P, TC], i32)
        last_window = sb("last_window", [P, TC])
        last_step = sb("last_step", [P, TC])
        reached = acc.ap().rearrange("p b d -> p (b d)")[:, 0:TC * KPAD].rearrange("p (c k) -> p c k", c=TC)
        rows_f = acc.ap().rearrange("p b d -> p (b d)")[:, 0:2 * TC * P].rearrange("p (e c j) -> p e c j", e=2, c=TC)

        window_iota = sb("window_iota", [P, WIN])
        ident = sb("ident", [P, P])
        ones = sb("ones", [P, P])

        stage = sb("stage", [P, RING, S], i32)
        rows = sb("rows", [P, RING, S, D])
        rows_mlp = sb("rows_mlp", [P, RING, S, MH])
        onehot = sb("onehot", [P, RING, S, WIN])
        onehot_b = sb("onehot_b", [P, HELD, S, WIN], bf16)
        onehot_t = sb("onehot_t", [P, 2, S, WB, P], bf16)
        window_iota_b = sb("window_iota_b", [P, WIN], bf16)
        ident_b = sb("ident_b", [P, P], bf16)
        new_weight = sb("new_weight", [P, 2, S])
        rest = sb("rest", [P, 2, S])
        weight_parts = sb("weight_parts", [P, 2, S, PARTS + 1], bf16)
        pre = sb("pre", [P, 2, S, MH])
        gelu = sb("gelu", [P, 2, S, MH])
        scaled = sb("scaled", [P, 2, S, MH])
        logit = sb("logit", [P, 2, S])
        tanh_half = sb("tanh_half", [P, 2, S])

        chunk = sb("chunk", [P, 2, CB, D])
        chunk_t = sb("chunk_t", [P, 2, CN])
        hidden = sb("hidden", [P, 2, CN])
        stats = sb("stats", [P, CB, nc.vector.BN_STATS_DIM])
        moments = sb("moments", [P, CB, nc.vector.BN_AGGR_DIM])
        rstd = sb("rstd", [P, CB])
        dst_rest = sb("dst_rest", [P, CB, MH])
        src_mlp = sb("src_mlp", [P, CB, MH])

        w_mlp_cat = sb("w_mlp_cat", [P, 2 * MH])
        w_conv = {n: sb("w_" + n, [P, D]) for n in ("L0_gnn_conv_w", "L3_gnn_W0", "L3_gnn_W1", "L3_gnn_W2")}
        w_up = {n: sb("w_" + n, [P, HID]) for n in ("L1_gnn_W1", "L2_gnn_Wm1")}
        w_up2 = sb("w_L2_gnn_Wn1", [P, 2, HID])
        w_down = {n: sb("w_" + n, [P, 2, D]) for n in ("L1_gnn_W2", "L2_gnn_Wm2", "L2_gnn_Wn2")}
        b_row = {n: sb("b_" + n, [P, D]) for n in ("L0_gnn_conv_b", "L1_gnn_b2", "L2_gnn_bm2", "L2_gnn_bn2",
                                                   "L3_gnn_b0", "L3_gnn_b1", "L3_gnn_b2")}
        b_col = {n: sb("b_" + n, [P, 2]) for n in ("L1_gnn_b1", "L2_gnn_bm1", "L2_gnn_bn1")}
        b_mlp1 = sb("b_mlp1", [P, MH])
        w_mlp2 = sb("w_mlp2", [P, MH])
        b_mlp2 = sb("b_mlp2", [P, 1])
        half_b2 = sb("half_b2", [P, 1])

        ps = ctx.enter_context(nc.psum_tensor("ps", [P, 4096], f32))
        BANK = 512
        products = ps[:, :].rearrange("p (r s w d) -> p r s w d", r=RING, s=S, w=WB)
        ps_onehot_t = ps[:, 0:2 * BANK].bitcast(bf16).rearrange("p (r s w e) -> p r s w e", r=2, s=S, w=WB)
        ps_mlp = ps[:, 4 * BANK:6 * BANK].rearrange("p (r s m) -> p r s m", r=2, m=MH)
        ps_deg = ps[:, 6 * BANK:8 * BANK].rearrange("p (r n) -> p r n", r=2)[:, :, 0:S * WB * (PARTS + 1)].rearrange(
            "p r (s w c) -> p r s w c", s=S, w=WB)
        ps_t = ps[:, 0:CN]
        ps_out = ps[:, 2 * BANK:2 * BANK + CN].rearrange("p (b d) -> p b d", b=CB)
        HALF = CN // 2
        ps_hidden = ps[:, 4 * BANK:8 * BANK].rearrange("p (h c n) -> p h c n", h=2, c=2)[:, :, :, 0:HALF]
        ps_tile_halves = ps[:, 0:2 * BANK].rearrange("p (h k) -> p h k", h=2)[:, :, 0:KPAD // 2]
        ps_tile_t = ps[:, 2 * BANK:2 * BANK + TC]
        ps_edges = ps[:, 3 * BANK:3 * BANK + 2 * TC * P].rearrange("p (e k) -> p e k", e=2)

        def signals(name):
            return dict(
                fed=sem(name + "_fed"),
                turned=sem(name + "_turned"),
                turned_sb=sem(name + "_turned_sb"),
                upped=sem(name + "_upped"),
                upped_sb=sem(name + "_upped_sb"),
                multiplied=sem(name + "_multiplied"),
                taken=sem(name + "_taken"),
                written=sem(name + "_written"),
                stored=sem(name + "_stored"),
                variances=sem(name + "_variances"),
                roots=sem(name + "_roots"),
                own_pre=sem(name + "_own_pre"),
                own_post=sem(name + "_own_post"),
            )

        MLP = dict(signals("mlp"), sources=1, turned_as="relu", conv=w_mlp_cat)
        CONV0 = dict(signals("conv0"), sources=1, conv=w_conv["L0_gnn_conv_w"])
        GCN1 = dict(signals("gcn1"), sources=1, up=w_up["L1_gnn_W1"], up_b=b_col["L1_gnn_b1"], down=w_down["L1_gnn_W2"])
        MESSAGE = dict(signals("message"), sources=1, turned_as="relu", up=w_up["L2_gnn_Wm1"], up_b=b_col["L2_gnn_bm1"], down=w_down["L2_gnn_Wm2"])
        UPDATE = dict(signals("update"), sources=2, up=w_up2, up_b=b_col["L2_gnn_bn1"], down=w_down["L2_gnn_Wn2"])
        GCN3A = dict(signals("gcn3a"), sources=1, conv=w_conv["L3_gnn_W0"])
        GCN3B = dict(signals("gcn3b"), sources=1, conv=w_conv["L3_gnn_W1"])
        GCN3C = dict(signals("gcn3c"), sources=1, conv=w_conv["L3_gnn_W2"])
        for one in (GCN1, MESSAGE):
            one["taken"] = one["written"]
        DENSE = [MLP, CONV0, GCN1, MESSAGE, UPDATE, GCN3A, GCN3B, GCN3C]
        FILLS = {0: MLP, 2: CONV0, 3: GCN1, 4: MESSAGE, 5: UPDATE, 6: GCN3A, 7: GCN3B}

        pads_set = sem("pads_set")
        rows_in = sem("rows_in")
        lists_stored = sem("lists_stored")
        iotas = sem("iotas")
        prep = sem("prep")
        reached_set = sem("reached_set")
        tiles_counted = sem("tiles_counted")
        tile_of_set = sem("tile_of_set")
        steps_in = sem("steps_in")
        rows_f_set = sem("rows_f_set")
        edges_turned = sem("edges_turned")
        steps_set = sem("steps_set")
        x_pad_set = sem("x_pad_set")
        x_in = sem("x_in")
        weights_in = sem("weights_in")
        table1_set = sem("table1_set")
        table1_stored = sem("table1_stored")
        acc_cleared = sem("acc_cleared")
        passed = sem("passed")
        inverses = sem("inverses")

        degree_roots = sem("degree_roots")

        staged = sem("staged")
        claimed = sem("claimed")
        gathered = [sem(f"gathered{j}") for j in range(RING)]
        onehots = sem("onehots")
        summed = sem("summed")
        added = sem("added")
        adding = sem("adding")
        e_turned = sem("e_turned")
        e_turned_sb = sem("e_turned_sb")
        e_dst = sem("e_dst")
        e_pre = sem("e_pre")
        e_gelu = sem("e_gelu")
        e_scaled = sem("e_scaled")
        e_logit = sem("e_logit")
        e_tanh = sem("e_tanh")
        splitting = sem("splitting")
        e_weight = sem("e_weight")

        LOADS = 2 + len(w_conv) + len(w_up) + len(w_down) + 1 + len(b_row) + 2 * len(b_col) + 3
        block = ctx.enter_context(nc.Block())

        def rows_gathered(eng, p, g, j):
            j = j % RING
            turn = g // RING if isinstance(g, int) else (g - j) // RING
            eng.wait_ge(gathered[j], (turn + (p * USES[j] + 1)) * (16 * S))

        def rows_read(eng, p, g):
            if p == 0:
                after(eng, e_pre, g - RING + 1)
            else:
                after(eng, summed, g + (p * GROUPS - RING + 1))

        def windows(g, engine):
            at = window_of[0:1, bass.ds(g * S, S)]
            return nc.values_load_multi_w_load_instructions(
                at, engines=[engine], min_val=0, max_val=NW - 1,
                skip_runtime_bounds_check_because="a step's window is at most the last one, as the merge path has it")[1]

        @block.sync
        def _(sp):
            full = (TC - 1) * P
            rest = E // P - full
            whole = N // P
            sp.dma_start(x[:, 0:whole, :], a["x"][0:whole * P, :].rearrange("(b p) d -> p b d", p=P)).then_inc(x_in, 16)
            for e, name in enumerate(("src", "dst")):
                sp.dma_start(rows_i[:, e, 0:TC - 1, :],
                             a[name][0:full * P].rearrange("(c p j) -> p c j", p=P, j=P)).then_inc(rows_in, 16)
            sp.wait_ge(pads_set, 2)
            for e, name in enumerate(("src", "dst")):
                sp.dma_start(rows_i[0:rest, e, TC - 1, :],
                             a[name][full * P:(full + rest) * P].rearrange("(p j) -> p j", j=P)).then_inc(rows_in, 16)
                sp.dma_start(rows_i[rest:rest + 1, e, TC - 1, 0:E % P],
                             a[name][(full + rest) * P:E].rearrange("(p j) -> p j", p=1)).then_inc(rows_in, 16)
            sp.wait_ge(x_pad_set, 1)
            sp.dma_start(x[0:N % P, whole, :], a["x"][whole * P:N, :]).then_inc(x_in, 16)
            sp.wait_ge(rows_in, 16 * 6)
            for e in range(2):
                sp.dma_start(edge_list[e].rearrange("(c p) j -> p c j", p=P), rows_i[:, e, :, :]).then_inc(lists_stored, 16)

            def store(p, where, source):
                def item(i, _):
                    after(sp, p["written"], i + 1)
                    sp.dma_start(where[bass.ds(i * CN, CN), :].rearrange("(b p) d -> p b d", p=P),
                                 source(i)).then_inc(p["stored"], 16)
                return item

            for p in range(PASSES):
                if p == 1:
                    sp.wait_ge(table1_set, 1)
                    sp.dma_start(table[1].rearrange("(b p) d -> p b d", p=P), acc[:, :, :]).then_inc(table1_stored, 16)
                else:
                    source = (lambda i: src_mlp[:, :, :]) if p == 0 else (lambda i: acc[:, bass.ds(i * CB, CB), :])
                    pipeline(sp, NC, 1, [(0, store(FILLS[p], table[p], source))])
            pipeline(sp, NC - 1, 1, [(0, store(GCN3C, out, lambda i: x[:, bass.ds(i * CB, CB), :]))])
            sp.wait_ge(GCN3C["written"], NC)
            done = (NC - 1) * CB
            sp.dma_start(out[done * P:whole * P, :].rearrange("(b p) d -> p b d", p=P), x[:, done:whole, :]).then_inc(GCN3C["stored"], 16)
            sp.dma_start(out[whole * P:N, :], x[0:N % P, whole, :]).then_inc(GCN3C["stored"], 16)
            for p in DENSE[:-1]:
                sp.wait_ge(p["stored"], 16 * NC)
            sp.wait_ge(table1_stored, 16)
            sp.wait_ge(lists_stored, 32)
            sp.wait_ge(GCN3C["stored"], 16 * (NC + 1))

        @block.gpsimd
        def _(pool):
            nc.gpsimd.iota(step_iota[:, :], [[1, KPAD]], base=0, channel_multiplier=0,
                           allow_small_or_imprecise_dtypes=True).then_inc(iotas, 1)
            nc.gpsimd.iota(tile_iota[:, :], [[P, TC]], base=0, channel_multiplier=1,
                           allow_small_or_imprecise_dtypes=True).then_inc(iotas, 1)
            nc.gpsimd.iota(window_iota[:, :], [[1, WIN]], base=0, channel_multiplier=0,
                           allow_small_or_imprecise_dtypes=True).then_inc(iotas, 1)
            nc.gpsimd.memset(ones[:, :], 1.0).then_inc(iotas, 1)
            pool.wait_ge(iotas, 4)
            nc.gpsimd.affine_select(out=ident[:, :], in_=ones[:, :], compare_op=ALU.is_equal, fill=0.0, base=0,
                                    pattern=[[-1, P]], channel_multiplier=1).then_inc(iotas, 1)
            pool.wait_ge(iotas, 5)
            nc.gpsimd.tensor_copy(ident_b[:, :], ident[:, :]).then_inc(iotas, 1)
            nc.gpsimd.tensor_copy(window_iota_b[:, :], window_iota[:, :]).then_inc(iotas, 1)
            pool.wait_ge(tile_of_set, 1)
            pool.wait_ge(lists_stored, 32)
            for e in range(2):
                for c in range(TC):
                    nc.gpsimd.indirect_dma_start(out=rows_i[:, e, c, :], out_offset=None, in_=edge_list[e][:, :],
                                                 in_offset=bass.IndirectOffsetOnAxis(ap=tile_of[:, c:c + 1], axis=0)).then_inc(steps_in, 16)

            def gather(p):
                def item(g, j):
                    after(pool, staged, g + (p * GROUPS + 1))
                    rows_read(pool, p, g)
                    pool.sem_inc(claimed, 1)
                    where = rows_mlp if p == 0 else rows
                    for s in range(S):
                        nc.gpsimd.indirect_dma_start(out=where[:, j, s, :], out_offset=None, in_=table[p][:, :],
                                                     in_offset=bass.IndirectOffsetOnAxis(ap=stage[:, j, s:s + 1], axis=0)).then_inc(gathered[j], 16)
                return item

            for p in range(PASSES):
                pool.wait_ge(*((table1_stored, 16) if p == 1 else (FILLS[p]["stored"], 16 * NC)))
                pipeline(pool, GROUPS, RING, [(0, gather(p))])

        @block.scalar
        def _(act):
            loads = [(w_mlp_cat[:, 0:MH], a["L0_gnn_mlp_w1"][0:D, :]), (w_mlp_cat[:, MH:2 * MH], a["L0_gnn_mlp_w1"][D:2 * D, :])]
            loads += [(w[:, :], a[n][:, :]) for n, w in list(w_conv.items()) + list(w_up.items())]
            loads += [(w[:, :, :], a[n].rearrange("(h p) d -> p h d", p=P)) for n, w in list(w_down.items()) + [("L2_gnn_Wn1", w_up2)]]
            loads += [(b[:, :], a[n].partition_broadcast(P)) for n, b in b_row.items()]
            loads += [(b[:, k:k + 1], a[n][k * P:(k + 1) * P].rearrange("(p o) -> p o", o=1)) for n, b in b_col.items() for k in range(2)]
            loads += [(b_mlp1[:, :], a["L0_gnn_mlp_b1"].partition_broadcast(P)),
                      (w_mlp2[:, :], a["L0_gnn_mlp_w2"].rearrange("m o -> (m o)").partition_broadcast(P)),
                      (b_mlp2[:, :], a["L0_gnn_mlp_b2"].partition_broadcast(P))]
            for where, source in loads:
                act.dma_start(where, source).then_inc(weights_in, 16)

            def dense(p):
                sources = p["sources"]

                def copy_turned(i, _):
                    for n in range(sources):
                        after(act, p["turned"], i * sources + n + 1)
                        after(act, p["upped"] if "up" in p else p["multiplied"], i)
                        if p.get("turned_as") == "relu":
                            nc.scalar.activation(chunk_t[:, n, :], ps_t, ACT.Relu).then_inc(p["turned_sb"], 1)
                        else:
                            nc.scalar.copy(chunk_t[:, n, :], ps_t).then_inc(p["turned_sb"], 1)

                def relu_hidden(i, _):
                    after(act, p["upped"], i + 1)
                    after(act, p["multiplied"], i)
                    for half in range(2):
                        last = nc.scalar.activation(hidden[:, half, :].rearrange("p (c n) -> p c n", c=2), ps_hidden[:, half],
                                                    ACT.Relu, bias=p["up_b"][:, half:half + 1])
                    last.then_inc(p["upped_sb"], 1)

                def take_roots(i, _):
                    after(act, p["variances"], i + 1)
                    nc.scalar.activation(rstd[:, :], rstd[:, :], ACT.Sqrt).then_inc(p["roots"], 1)

                stages = [(0, take_roots)] if p in (MLP, MESSAGE) else []
                stages.append((0, copy_turned))
                if "up" in p:
                    stages.append((1 if sources == 1 else 0, relu_hidden))
                if p in (CONV0, UPDATE):
                    stages.append((1, take_roots))
                pipeline(act, NC, 1, stages)

            def stage_indices(p):
                def item(g, j):
                    rows_read(act, p, g)
                    nc.scalar.copy(stage[:, j, :], src_of[:, bass.ds(g * S, S)]).then_inc(staged, 1)
                return item

            def copy_onehot(g, j):
                after(act, e_turned, g + 1)
                after(act, e_dst, g - 1)
                nc.scalar.copy(onehot_t[:, j % 2], ps_onehot_t[:, j % 2]).then_inc(e_turned_sb, 1)

            def gelu_group(g, j):
                after(act, e_pre, g + 1)
                after(act, e_scaled, g - 1)
                nc.scalar.activation(gelu[:, j % 2], pre[:, j % 2], ACT.Gelu).then_inc(e_gelu, 1)

            def tanh_group(g, j):
                after(act, e_logit, g + 1)
                after(act, e_weight, g - 1)
                nc.scalar.activation(tanh_half[:, j % 2], logit[:, j % 2], ACT.Tanh, bias=half_b2[:, 0:1],
                                     scale=0.5).then_inc(e_tanh, 1)

            act.wait_ge(weights_in, 16 * LOADS)
            dense(MLP)
            act.wait_ge(steps_set, 1)
            pipeline(act, GROUPS, RING, [(0, stage_indices(0)), (1, copy_onehot), (3, tanh_group), (2, gelu_group)])
            act.wait_ge(inverses, PARTS)
            nc.scalar.activation(dinv[:, :, :], dinv[:, :, :], ACT.Sqrt).then_inc(degree_roots, 1)
            for p in range(1, PASSES):
                pipeline(act, GROUPS, RING, [(0, stage_indices(p))])
                dense(DENSE[p])

        @block.tensor
        def _(pe):
            pe.wait_ge(iotas, 7)
            pe.wait_ge(reached_set, 1)
            for k0 in range(0, KPAD, KPAD // 2):
                for c in range(TC):
                    nc.tensor.matmul(ps_tile_halves[:, k0 // (KPAD // 2), :], ones[:, :], reached[:, c, k0:k0 + KPAD // 2],
                                     start=(c == 0), stop=(c == TC - 1))
            for k in range(TC):
                for c in range(TC):
                    last = nc.tensor.matmul(ps_tile_t[:, k:k + 1], reached[:, c, k * P:(k + 1) * P], ones[:, 0:1],
                                            start=(c == 0), stop=(c == TC - 1))
            last.then_inc(tiles_counted, 1)
            pe.wait_ge(rows_f_set, 1)
            for e in range(2):
                for c in range(TC):
                    last = nc.tensor.transpose(ps_edges[:, e, c * P:(c + 1) * P], rows_f[:, e, c, :], ident[:, :])
            last.then_inc(edges_turned, 1)

            def dense(p):
                sources = p["sources"]

                def turn(i, _):
                    after(pe, p["fed"], i + 1)
                    for n in range(sources):
                        after(pe, p["turned_sb"], i * sources + n)
                        for b in range(CB):
                            last = nc.tensor.transpose(ps_t[:, b * P:(b + 1) * P], chunk[:, n, b, :], ident[:, :])
                        last.then_inc(p["turned"], 1)

                def multiply(i, _):
                    after(pe, p["turned_sb"], (i + 1) * sources)
                    if "up" in p:
                        after(pe, p["upped_sb"], i)
                        for half in range(2):
                            for c in range(2):
                                for n in range(sources):
                                    w = p["up"][:, n, half * P:(half + 1) * P] if sources > 1 else p["up"][:, half * P:(half + 1) * P]
                                    last = nc.tensor.matmul(ps_hidden[:, half, c, :], w, chunk_t[:, n, c * HALF:(c + 1) * HALF],
                                                            start=(n == 0), stop=(n == sources - 1))
                        last.then_inc(p["upped"], 1)
                        after(pe, p["upped_sb"], i + 1)
                    after(pe, p["taken"], i)
                    for b in range(CB):
                        if "up" in p:
                            for half in range(2):
                                last = nc.tensor.matmul(ps_out[:, b, :], hidden[:, half, b * P:(b + 1) * P], p["down"][:, half, :],
                                                        start=(half == 0), stop=(half == 1))
                        else:
                            last = nc.tensor.matmul(ps_out[:, b, :], chunk_t[:, 0, b * P:(b + 1) * P], p["conv"][:, :],
                                                    start=True, stop=True)
                    last.then_inc(p["multiplied"], 1)

                pipeline(pe, NC, 1, [(0, turn), (1 if sources == 1 else 0, multiply)])

            def turn_onehots(g, j):
                after(pe, onehots, g + 1)
                after(pe, e_turned_sb, g - 1)
                for s in range(S):
                    for w in range(WB):
                        last = nc.tensor.transpose(ps_onehot_t[:, j % 2, s, w, :], onehot_b[:, j, s, w * P:(w + 1) * P], ident_b[:, :])
                last.then_inc(e_turned, 1)

            def dst_half(g, j):
                window = windows(g, ENG.PE)
                after(pe, e_turned_sb, g + 1)
                after(pe, e_pre, g - 1)
                for s in range(S):
                    for w in range(WB):
                        for part in range(PARTS):
                            last = nc.tensor.matmul(ps_mlp[:, j % 2, s, :], onehot_t[:, j % 2, s, w, :],
                                                    dst_mlp[:, bass.ds(window[s] * WB + w, 1), part, :].rearrange("p o m -> p (o m)"),
                                                    start=(w == 0 and part == 0), stop=(w == WB - 1 and part == PARTS - 1))
                last.then_inc(e_dst, 1)

            def sum_degrees(g, j):
                after(pe, e_weight, g + 1)
                after(pe, added, g - 1)
                for s in range(S):
                    for w in range(WB):
                        last = nc.tensor.matmul(ps_deg[:, j % 2, s, w, :], onehot_b[:, j, s, w * P:(w + 1) * P],
                                                weight_parts[:, j % 2, s, :], start=True, stop=True)
                last.then_inc(summed, 1)

            def sum_rows(p):
                def item(g, j):
                    after(pe, onehots, g + (p * GROUPS + 1))
                    after(pe, added, g + (p * GROUPS - RING + 1))
                    rows_gathered(pe, p, g, j)
                    for s in range(S):
                        for w in range(WB):
                            last = nc.tensor.matmul(products[:, j, s, w, :], onehot[:, j, s, w * P:(w + 1) * P], rows[:, j, s, :],
                                                    start=True, stop=True)
                    last.then_inc(summed, 1)
                return item

            pe.wait_ge(weights_in, 16 * LOADS)
            pe.wait_ge(steps_set, 1)
            dense(MLP)
            pe.wait_ge(MLP["taken"], NC)
            pipeline(pe, GROUPS, HELD, [(4, sum_degrees), (1, dst_half), (0, turn_onehots)])
            for p in range(1, PASSES):
                if p > 1:
                    pe.wait_ge(DENSE[p - 1]["taken"], NC)
                pe.wait_ge(added, p * GROUPS)
                pipeline(pe, GROUPS, RING, [(0, sum_rows(p))])
                pe.wait_ge(added, (p + 1) * GROUPS)
                dense(DENSE[p])

        @block.vector
        def _(dve):
            made = [0]

            def link(instruction):
                made[0] += 1
                instruction.then_inc(prep, 1)
                dve.wait_ge(prep, made[0])

            nc.vector.memset(rows_i[:, 0, TC - 1, :], 0).then_inc(pads_set, 1)
            nc.vector.memset(rows_i[:, 1, TC - 1, :], FAR).then_inc(pads_set, 1)
            nc.vector.memset(x[:, N // P:NB, :], 0.0).then_inc(x_pad_set, 1)
            nc.vector.memset(deg[:, :, :], 0.0)
            link(nc.vector.memset(weight_parts[:, :, :, :], 1.0))

            dve.wait_ge(rows_in, 16 * 6)
            link(nc.vector.tensor_scalar(last_window_i[:, :], rows_i[:, 1, :, P - 1], WIN_SHIFT, None, ALU.arith_shift_right))
            link(nc.vector.tensor_copy(last_window[:, :], last_window_i[:, :]))
            dve.wait_ge(iotas, 7)
            link(nc.vector.scalar_tensor_tensor(last_step[:, :], last_window[:, :], float(NW - 1), tile_iota[:, :],
                                                ALU.min, ALU.add))
            for c in range(TC):
                last = nc.vector.tensor_scalar(reached[:, c, :], step_iota[:, :], last_step[:, c:c + 1], None, ALU.is_gt)
            last.then_inc(reached_set, 1)
            dve.wait_ge(tiles_counted, 1)
            nc.vector.tensor_copy(tile_of[:, :], ps_tile_t).then_inc(tile_of_set, 1)
            link(nc.vector.tensor_tensor(window_f[:, :].rearrange("p (h k) -> p h k", h=2),
                                         step_iota[:, :].rearrange("p (h k) -> p h k", h=2), ps_tile_halves, ALU.subtract))
            nc.vector.tensor_copy(window_of[:, :], window_f[:, :])
            dve.wait_ge(steps_in, 16 * 2 * TC)
            nc.vector.tensor_copy(rows_f, rows_i[:, :, :, :]).then_inc(rows_f_set, 1)
            dve.wait_ge(edges_turned, 1)
            nc.vector.tensor_copy(src_of[:, :], ps_edges[:, 0, :])
            nc.vector.scalar_tensor_tensor(local_dst[:, :], window_f[:, :], -float(WIN), ps_edges[:, 1, :],
                                           ALU.mult, ALU.add).then_inc(steps_set, 1)
            dve.wait_ge(weights_in, 16 * LOADS)
            link(nc.vector.tensor_scalar(half_b2[:, :], b_mlp2[:, :], 0.5, None, ALU.mult))
            dve.wait_ge(x_in, 32)

            def some(t, i):
                return t[:, bass.ds(i * CB, CB), :]

            def inverse(n, i):
                return dinv[:, n, bass.ds(i * CB, CB)].unsqueeze(2).to_broadcast([P, CB, D])

            def row(b, m=D):
                return b[:, :].unsqueeze(1).to_broadcast([P, CB, m])

            def normalize(p, i, own, into=None):
                dve.sem_inc(passed, 1)
                for b in range(CB):
                    last = nc.vector.bn_stats(stats[:, b, :], x[:, bass.ds(i * CB + b, 1), :].rearrange("p o d -> p (o d)"))
                own.done(last)
                own.wait()
                dve.sem_inc(passed, 1)
                for b in range(CB):
                    last = nc.vector.bn_aggr(moments[:, b, :], stats[:, b, :])
                own.done(last)
                own.wait()
                nc.vector.tensor_scalar(rstd[:, :], moments[:, :, 1], EPS, None, ALU.add).then_inc(p["variances"], 1)
                after(dve, p["roots"], i + 1)
                own.done(nc.vector.reciprocal(rstd[:, :], rstd[:, :]))
                own.wait()
                for b in range(CB):
                    last = nc.vector.tensor_scalar(into[:, b, :] if into is not None else h[:, bass.ds(i * CB + b, 1), :].rearrange("p o d -> p (o d)"),
                                                   x[:, bass.ds(i * CB + b, 1), :].rearrange("p o d -> p (o d)"),
                                                   moments[:, b, 0:1], rstd[:, b:b + 1], ALU.subtract, ALU.mult)
                own.done(last)
                own.wait()

            def chunks(p, pre_item, post_item):
                own_pre, own_post = Own(dve, p["own_pre"]), Own(dve, p["own_post"])

                def pre_stage(i, _):
                    own_pre.item(i)
                    pre_item(i, own_pre)

                def post_stage(i, _):
                    own_post.item(i)
                    after(dve, p["multiplied"], i + 1)
                    post_item(i, own_post)
                pipeline(dve, NC, 1, [(0, pre_stage), (1, post_stage)])

            def take(p, i, instruction):
                instruction.then_inc(p["taken"], 1)
                after(dve, p["taken"], i + 1)

            def scale_sums(p, n):
                def pre_item(i, own):
                    after(dve, p["turned"], i)
                    nc.vector.tensor_tensor(chunk[:, 0], some(acc, i), inverse(n, i), ALU.mult).then_inc(p["fed"], 1)
                return pre_item

            def add_to_x(p, i, own, bias):
                take(p, i, nc.vector.tensor_tensor(some(x, i), some(x, i), ps_out, ALU.add))
                own.done(nc.vector.tensor_tensor(some(x, i), some(x, i), row(bias), ALU.add))
                own.wait()

            def next_table(p, i):
                nc.vector.scalar_tensor_tensor(some(acc, i), some(h, i), 0.0, inverse(1, i), ALU.max, ALU.mult).then_inc(p["written"], 1)

            def mlp_pre(i, own):
                after(dve, MLP["turned"], i)
                normalize(MLP, i, own, chunk[:, 0])
                nc.vector.tensor_scalar(some(h, i), chunk[:, 0], 0.0, None, ALU.max).then_inc(MLP["fed"], 1)

            def mlp_post(i, own):
                after(dve, MLP["stored"], i * 16)
                nc.vector.tensor_tensor(src_mlp[:, :, :], ps_out[:, :, 0:MH], row(b_mlp1, MH), ALU.add).then_inc(MLP["written"], 1)
                own.done(nc.vector.tensor_copy(dst_rest[:, :, :], ps_out[:, :, MH:2 * MH]))
                own.wait()
                for part in range(PARTS):
                    to = dst_mlp[:, bass.ds(i * CB, CB), part, :]
                    if part < PARTS - 1:
                        own.done(nc.vector.tensor_copy(to, dst_rest[:, :, :]))
                        own.wait()
                        own.done(nc.vector.tensor_tensor(dst_rest[:, :, :], dst_rest[:, :, :], to, ALU.subtract))
                        own.wait()
                    else:
                        nc.vector.tensor_copy(to, dst_rest[:, :, :]).then_inc(MLP["taken"], 1)

            chunks(MLP, mlp_pre, mlp_post)

            def write_onehots(p):
                def item(g, j):
                    held = HELD if p == 0 else RING
                    after(dve, summed, g + (p * GROUPS - held + 1))
                    to, iota = (onehot_b, window_iota_b) if p == 0 else (onehot, window_iota)
                    for s in range(S):
                        k = g * S + s
                        how = dict(scalar2=weight[:, bass.ds(k, 1)], op1=ALU.mult) if p == 1 else dict(scalar2=None)
                        last = nc.vector.tensor_scalar(to[:, j, s, :], iota[:, :], local_dst[:, bass.ds(k, 1)],
                                                       op0=ALU.is_equal, **how)
                    last.then_inc(onehots, 1)
                return item

            def add_products(p):
                def item(g, j):
                    window = windows(g, ENG.DVE)
                    after(dve, summed, g + (p * GROUPS + 1))
                    for s in range(S):
                        if s:
                            after(dve, adding, (g + p * GROUPS) * (S - 1) + s)
                        else:
                            after(dve, added, g + p * GROUPS)
                        to = (deg if p == 0 else acc)[:, bass.ds(window[s] * WB, WB), :]
                        source = ps_deg[:, j % 2, s] if p == 0 else products[:, j, s]
                        nc.vector.tensor_tensor(to, to, source, ALU.add).then_inc(added if s == S - 1 else adding, 1)
                return item

            def add_halves(g, j):
                after(dve, e_dst, g + 1)
                after(dve, e_gelu, g - 1)
                rows_gathered(dve, 0, g, j)
                nc.vector.tensor_tensor(pre[:, j % 2], ps_mlp[:, j % 2, 0:S, :], rows_mlp[:, j % RING], ALU.add).then_inc(e_pre, 1)

            def reduce_logits(g, j):
                after(dve, e_gelu, g + 1)
                nc.vector.tensor_tensor(scaled[:, j % 2], gelu[:, j % 2], w_mlp2[:, :].unsqueeze(1).to_broadcast([P, S, MH]),
                                        ALU.mult).then_inc(e_scaled, 1)
                after(dve, e_scaled, g + 1)
                after(dve, e_tanh, g - 1)
                nc.vector.tensor_reduce(logit[:, j % 2], scaled[:, j % 2], AX.X, ALU.add).then_inc(e_logit, 1)

            def write_weights(g, j):
                after(dve, e_tanh, g + 1)
                now, left, parts = new_weight[:, j % 2], rest[:, j % 2], weight_parts[:, j % 2]
                nc.vector.tensor_scalar(now, tanh_half[:, j % 2], 0.5, 0.5, ALU.mult, ALU.add).then_inc(splitting, 1)
                dve.wait_ge(splitting, g * 4 + 1)
                nc.vector.tensor_copy(weight[:, bass.ds(g * S, S)], now)
                after(dve, summed, g - 1)
                nc.vector.tensor_copy(parts[:, :, 0], now).then_inc(splitting, 1)
                dve.wait_ge(splitting, g * 4 + 2)
                nc.vector.tensor_tensor(left, now, parts[:, :, 0], ALU.subtract).then_inc(splitting, 1)
                dve.wait_ge(splitting, g * 4 + 3)
                nc.vector.tensor_copy(parts[:, :, 1], left).then_inc(splitting, 1)
                dve.wait_ge(splitting, g * 4 + 4)
                nc.vector.tensor_tensor(parts[:, :, 2], left, parts[:, :, 1], ALU.subtract).then_inc(e_weight, 1)

            dve.wait_ge(steps_set, 1)
            pipeline(dve, GROUPS, HELD, [(5, add_products(0)), (4, write_weights), (3, reduce_logits), (2, add_halves),
                                         (0, write_onehots(0))])
            dve.wait_ge(added, GROUPS)
            for part in range(1, PARTS):
                nc.vector.tensor_tensor(deg[:, :, 0], deg[:, :, 0], deg[:, :, part], ALU.add).then_inc(inverses, 1)
                dve.wait_ge(inverses, part)
            both = deg[:, :, 0:PARTS + 1:PARTS].rearrange("p b c -> p c b")
            nc.vector.tensor_scalar(deg_ok[:, :, :], both, 1.0, 0.0, ALU.add, ALU.is_gt)
            nc.vector.tensor_scalar(dinv[:, :, :], both, 1.0, 1e-30, ALU.add, ALU.max).then_inc(inverses, 1)
            dve.wait_ge(degree_roots, 1)
            nc.vector.reciprocal(dinv[:, :, :], dinv[:, :, :]).then_inc(inverses, 1)
            dve.wait_ge(inverses, PARTS + 1)
            nc.vector.tensor_tensor(dinv[:, :, :], dinv[:, :, :], deg_ok[:, :, :], ALU.mult).then_inc(inverses, 1)
            dve.wait_ge(inverses, PARTS + 2)
            nc.vector.tensor_tensor(acc[:, :, :], h[:, :, :], dinv[:, 0, :].unsqueeze(2).to_broadcast([P, NB, D]),
                                    ALU.mult).then_inc(table1_set, 1)
            dve.wait_ge(table1_stored, 16)

            def aggregate(p):
                pipeline(dve, GROUPS, RING, [(0, write_onehots(p)), (1, add_products(p))])
                dve.wait_ge(added, (p + 1) * GROUPS)

            aggregate(1)

            def conv0_post(i, own):
                add_to_x(CONV0, i, own, b_row["L0_gnn_conv_b"])
                normalize(CONV0, i, own)
                next_table(CONV0, i)

            chunks(CONV0, scale_sums(CONV0, 0), conv0_post)
            dve.wait_ge(CONV0["stored"], 16 * NC)
            aggregate(2)

            def gcn1_post(i, own):
                nc.vector.tensor_tensor(some(acc, i), ps_out, inverse(1, i), ALU.mult).then_inc(GCN1["written"], 1)

            chunks(GCN1, scale_sums(GCN1, 1), gcn1_post)
            dve.wait_ge(GCN1["stored"], 16 * NC)
            aggregate(3)

            def message_pre(i, own):
                after(dve, MESSAGE["turned"], i)
                own.done(nc.vector.tensor_tensor(chunk[:, 0], some(acc, i), inverse(1, i), ALU.mult))
                own.wait()
                own.done(nc.vector.tensor_tensor(chunk[:, 0], chunk[:, 0], row(b_row["L1_gnn_b2"]), ALU.add))
                own.wait()
                own.done(nc.vector.scalar_tensor_tensor(some(x, i), chunk[:, 0], 0.0, some(x, i), ALU.max, ALU.add))
                own.wait()
                normalize(MESSAGE, i, own, chunk[:, 0])
                nc.vector.tensor_scalar(some(h, i), chunk[:, 0], 0.0, None, ALU.max).then_inc(MESSAGE["fed"], 1)

            def message_post(i, own):
                nc.vector.tensor_tensor(some(acc, i), ps_out, row(b_row["L2_gnn_bm2"]), ALU.add).then_inc(MESSAGE["written"], 1)

            chunks(MESSAGE, message_pre, message_post)
            dve.wait_ge(MESSAGE["stored"], 16 * NC)
            nc.vector.memset(acc[:, :, :], 0.0).then_inc(acc_cleared, 1)
            dve.wait_ge(acc_cleared, 1)
            aggregate(4)

            def update_pre(i, own):
                after(dve, UPDATE["turned"], i * 2)
                nc.vector.tensor_copy(chunk[:, 0], some(h, i))
                nc.vector.tensor_copy(chunk[:, 1], some(acc, i)).then_inc(UPDATE["fed"], 1)

            def update_post(i, own):
                add_to_x(UPDATE, i, own, b_row["L2_gnn_bn2"])
                own.done(nc.vector.tensor_tensor(some(x, i), some(x, i), some(h, i), ALU.add))
                own.wait()
                normalize(UPDATE, i, own)
                next_table(UPDATE, i)

            chunks(UPDATE, update_pre, update_post)
            dve.wait_ge(UPDATE["stored"], 16 * NC)
            aggregate(5)

            for p, number, bias in ((GCN3A, 6, "L3_gnn_b0"), (GCN3B, 7, "L3_gnn_b1")):
                def gcn3_post(i, own, p=p, bias=bias):
                    take(p, i, nc.vector.tensor_tensor(some(h, i), ps_out, row(b_row[bias]), ALU.add))
                    next_table(p, i)

                chunks(p, scale_sums(p, 1), gcn3_post)
                dve.wait_ge(p["stored"], 16 * NC)
                aggregate(number)

            def gcn3c_post(i, own):
                take(GCN3C, i, nc.vector.tensor_tensor(some(x, i), some(x, i), ps_out, ALU.add))
                nc.vector.tensor_tensor(some(x, i), some(x, i), row(b_row["L3_gnn_b2"]), ALU.add).then_inc(GCN3C["written"], 1)

            chunks(GCN3C, scale_sums(GCN3C, 1), gcn3c_post)


def kernel(**inputs):
    import numpy as np
    import concourse.bacc as bacc
    from concourse.bass_utils import run_bass_kernel_spmd as run

    nc = bacc.Bacc("TRN2", target_bir_lowering=False, num_devices=1)
    arrays = {name: np.ascontiguousarray(v) for name, v in inputs.items()}
    aps = {name: nc.dram_tensor(f"in_{name}", v.shape, mybir.dt.from_np(v.dtype), kind="ExternalInput").ap()
           for name, v in arrays.items()}
    out = nc.dram_tensor("out", (N, D), mybir.dt.float32, kind="ExternalOutput").ap()
    build(nc, aps, out)
    r = run(nc, [{f"in_{name}": v for name, v in arrays.items()}], core_ids=[0])
    return r.results[0]["out"]
```
